# Optimizing a Trainium2 kernel written in Bass

```python
import numpy as np
import jax
import jax.numpy as jnp

def _softmax(x, axis=-1):
    return jax.nn.softmax(x, axis=axis)
def _gelu(x):
    return jax.nn.gelu(x, approximate=True)
def _silu(x):
    return jax.nn.silu(x)
def _sigmoid(x):
    return jax.nn.sigmoid(x)
def _layernorm(x, axis=-1, eps=1e-5):
    m = jnp.mean(x, axis=axis, keepdims=True)
    v = jnp.var(x, axis=axis, keepdims=True)
    return (x - m) / jnp.sqrt(v + eps)
def _scatter_add(tgt, idx, src, axis=0):
    return tgt.at[idx].add(src)
def _segment_sum(src, seg, n):
    return jax.ops.segment_sum(src, seg, n)

kernel_name = 'mk_rec_standalone_d1_rec_33904f'

def setup_inputs(seed: int = 0):
    np.random.seed(seed)
    _w = jnp.asarray
    def _rec_inputs():
        import jax
        import jax.numpy as jnp
        _rk = jax.random.key(seed)
        r_dense_features = -0.0115869 + 1.00573 * jax.random.normal(jax.random.fold_in(_rk, 1), (1024, 13), jnp.float32)
        r_sparse_features = jnp.stack([jax.random.randint(jax.random.fold_in(jax.random.fold_in(_rk, 2), 0), (1024,), 11, 10000, jnp.int32), jax.random.randint(jax.random.fold_in(jax.random.fold_in(_rk, 2), 1), (1024,), 1, 10000, jnp.int32), jax.random.randint(jax.random.fold_in(jax.random.fold_in(_rk, 2), 2), (1024,), 0, 9999, jnp.int32), jax.random.randint(jax.random.fold_in(jax.random.fold_in(_rk, 2), 3), (1024,), 5, 10000, jnp.int32), jax.random.randint(jax.random.fold_in(jax.random.fold_in(_rk, 2), 4), (1024,), 2, 9999, jnp.int32), jax.random.randint(jax.random.fold_in(jax.random.fold_in(_rk, 2), 5), (1024,), 2, 9998, jnp.int32), jax.random.randint(jax.random.fold_in(jax.random.fold_in(_rk, 2), 6), (1024,), 10, 9994, jnp.int32)], axis=1)
        return r_dense_features, r_sparse_features
    r_dense_features, r_sparse_features = _rec_inputs()
    def _L0_rec_setup():
        import jax, jax.numpy as jnp
        import numpy as np
        B = 2048
        D_DENSE = 13
        F = 7
        CARD = 10000
        E = 64
        D_OUT = 32
        S_OUT = 32
        D_HID = 2 * D_OUT
        S_HID = 2 * S_OUT
        CONCAT = D_OUT + F * S_OUT
        P_IN = CONCAT * CONCAT
        P_HID = 512
        key = jax.random.key(seed)
        ks = jax.random.split(key, 18)
        s = 0.05
        return {'dense_features': jax.random.normal(ks[0], (B, D_DENSE), dtype=jnp.float32), 'sparse_features': jax.random.randint(ks[1], (B, F), 0, CARD, dtype=jnp.int64), 'tokenizers': jnp.arange(CARD, dtype=jnp.int64), 'emb_tables': jax.random.normal(ks[2], (F, CARD, E), dtype=jnp.float32) * s, 'dw1': jax.random.normal(ks[3], (D_DENSE, D_HID), dtype=jnp.float32) * s, 'db1': jnp.zeros((D_HID,), dtype=jnp.float32), 'dw2': jax.random.normal(ks[4], (D_HID, D_OUT), dtype=jnp.float32) * s, 'db2': jnp.zeros((D_OUT,), dtype=jnp.float32), 'sw1': jax.random.normal(ks[5], (F, E, S_HID), dtype=jnp.float32) * s, 'sb1': jnp.zeros((F, S_HID), dtype=jnp.float32), 'sw2': jax.random.normal(ks[6], (F, S_HID, S_OUT), dtype=jnp.float32) * s, 'sb2': jnp.zeros((F, S_OUT), dtype=jnp.float32), 'pw1': jax.random.normal(ks[7], (P_IN, P_HID), dtype=jnp.float32) * s, 'pb1': jnp.zeros((P_HID,), dtype=jnp.float32), 'pw2': jax.random.normal(ks[8], (P_HID, 1), dtype=jnp.float32) * s, 'pb2': jnp.zeros((1,), dtype=jnp.float32)}
    _L0_rec_all = _L0_rec_setup()
    _L0_rec_in = {k: v for k, v in _L0_rec_all.items() if k in ('tokenizers', 'emb_tables', 'dw1', 'db1', 'dw2', 'db2', 'sw1', 'sb1', 'sw2', 'sb2', 'pw1', 'pb1', 'pw2', 'pb2', )}
    del _L0_rec_all

    return {
        "r_dense_features": r_dense_features,
        "r_sparse_features": r_sparse_features,
        "L0_rec_tokenizers": _L0_rec_in["tokenizers"],
        "L0_rec_emb_tables": _L0_rec_in["emb_tables"],
        "L0_rec_dw1": _L0_rec_in["dw1"],
        "L0_rec_db1": _L0_rec_in["db1"],
        "L0_rec_dw2": _L0_rec_in["dw2"],
        "L0_rec_db2": _L0_rec_in["db2"],
        "L0_rec_sw1": _L0_rec_in["sw1"],
        "L0_rec_sb1": _L0_rec_in["sb1"],
        "L0_rec_sw2": _L0_rec_in["sw2"],
        "L0_rec_sb2": _L0_rec_in["sb2"],
        "L0_rec_pw1": _L0_rec_in["pw1"],
        "L0_rec_pb1": _L0_rec_in["pb1"],
        "L0_rec_pw2": _L0_rec_in["pw2"],
        "L0_rec_pb2": _L0_rec_in["pb2"],
    }

def reference(r_dense_features, r_sparse_features, L0_rec_tokenizers, L0_rec_emb_tables, L0_rec_dw1, L0_rec_db1, L0_rec_dw2, L0_rec_db2, L0_rec_sw1, L0_rec_sb1, L0_rec_sw2, L0_rec_sb2, L0_rec_pw1, L0_rec_pb1, L0_rec_pw2, L0_rec_pb2):
    import jax
    import jax.numpy as jnp
    def _L0_rec_ref(dense_features, sparse_features, tokenizers, emb_tables, dw1, db1, dw2, db2, sw1, sb1, sw2, sb2, pw1, pb1, pw2, pb2):
        import jax, jax.numpy as jnp
        import numpy as np
        B = 2048
        D_DENSE = 13
        F = 7
        CARD = 10000
        E = 64
        D_OUT = 32
        S_OUT = 32
        D_HID = 2 * D_OUT
        S_HID = 2 * S_OUT
        CONCAT = D_OUT + F * S_OUT
        P_IN = CONCAT * CONCAT
        P_HID = 512
        dense_out = jnp.maximum(dense_features @ dw1 + db1, 0.0) @ dw2 + db2
        matches = sparse_features[:, :, None] == tokenizers[None, None, :]
        idx = jnp.argmax(matches, axis=2)
        gathered = emb_tables[jnp.arange(emb_tables.shape[0])[None, :], idx]
        h = jnp.maximum(jnp.einsum('bfe,feh->bfh', gathered, sw1) + sb1, 0.0)
        sparse_out = jnp.einsum('bfh,fho->bfo', h, sw2) + sb2
        concat = jnp.concatenate([dense_out, sparse_out.reshape(sparse_out.shape[0], -1)], axis=1)
        outer = jnp.einsum('bi,bj->bij', concat, concat)
        flattened = outer.reshape(concat.shape[0], -1)
        logits = jnp.maximum(flattened @ pw1 + pb1, 0.0) @ pw2 + pb2
        return jax.nn.sigmoid(logits).squeeze()

    y = _L0_rec_ref(r_dense_features, r_sparse_features, L0_rec_tokenizers, L0_rec_emb_tables, L0_rec_dw1, L0_rec_db1, L0_rec_dw2, L0_rec_db2, L0_rec_sw1, L0_rec_sb1, L0_rec_sw2, L0_rec_sb2, L0_rec_pw1, L0_rec_pb1, L0_rec_pw2, L0_rec_pb2)
    return y


_drawn_inputs = setup_inputs


def setup_inputs(seed=0):
    import zlib

    import numpy as np

    out = dict(_drawn_inputs(seed))
    spreads = {'L0_rec_db1': (0.0, 0.8),
     'L0_rec_db2': (0.0, 0.5),
     'L0_rec_sb1': (0.0, 0.8),
     'L0_rec_sb2': (0.0, 0.1),
     'L0_rec_pb1': (0.0, 0.601)}
    factors = {'r_dense_features': 5.045,
     'L0_rec_emb_tables': 8.0,
     'L0_rec_dw1': 5.487,
     'L0_rec_dw2': 5.428,
     'L0_rec_sw1': 8.0,
     'L0_rec_sw2': 2.789,
     'L0_rec_pw2': 3.244}
    for name, (base, spread) in spreads.items():
        noise = np.random.default_rng([zlib.crc32(name.encode()), seed]).standard_normal(out[name].shape)
        drawn = base * np.exp(spread * noise) if base else spread * noise
        out[name] = jnp.asarray(drawn.astype(out[name].dtype))
    for name, factor in factors.items():
        out[name] = (out[name] * factor).astype(out[name].dtype)
    return out
```

```python
from contextlib import ExitStack

import concourse.bass as bass
from concourse import mybir

ALU = mybir.AluOpType
ACT = mybir.ActivationFunctionType
AX_X = mybir.AxisListType.X
F32 = mybir.dt.float32
F32R = mybir.dt.float32r
I32 = mybir.dt.int32
U32 = mybir.dt.uint32
P = 128


def rec_kernel(nc, dense, sparse, tokens, emb, dw1, db1, dw2, db2, sw1, sb1, sw2, sb2, pw1, pb1, pw2, pb2, out):
    B, D_DENSE = dense.shape
    F, CARD, E = emb.shape
    S_OUT = sw2.shape[2]
    C = (F + 1) * S_OUT
    N_HID = pw1.shape[1]
    BT = B // P
    HALF = 512
    NH = B // HALF
    NT = N_HID // P
    PAIRS = (F + 1) // 2
    SLOT = E
    assert E == sw1.shape[2] == dw1.shape[1] and 2 * E == P and C == 2 * P and dw2.shape[1] == S_OUT
    assert NT * NH == 8 and BT * P == B

    LOOPED = [(m, k, 16) for m in (128, 64, 32) for k in range(m // 32)]
    TAIL = [(16, 0, 8), (8, 0, 4), (4, 0, 2), (2, 0, 1), (1, 0, 2)]
    ROUNDS = LOOPED + TAIL
    PER_ROUND = 16
    TAIL_AT = PER_ROUND * len(LOOPED)
    STEPS = sum(n for _, _, n in ROUNDS)
    SQUARES, LAST = STEPS - 2, STEPS - 1
    W_RING = 4
    CHUNK = 1000
    N_CHUNKS = CARD // CHUNK
    TOK_P = 80
    Q = BT * F
    assert CARD % CHUNK == 0 and CARD % TOK_P == 0 and STEPS == 129

    with ExitStack() as ctx:
        def sb(name, shape, dt=F32):
            return ctx.enter_context(nc.sbuf_tensor(name, shape, dt))

        def sem(name):
            return ctx.enter_context(nc.semaphore(name))

        c_dram = nc.dram_tensor("features_dram", (C, B), F32, kind="Internal")

        psum = ctx.enter_context(nc.psum_tensor("psum", [P, 8, HALF], F32))
        query = sb("query", [P, BT, F], I32)
        query_hi = sb("query_hi", [P, BT, F], I32)
        query_lo = sb("query_lo", [P, BT, F], I32)
        query_hi_f = sb("query_hi_f", [P, BT, F])
        query_lo_f = sb("query_lo_f", [P, BT, F])
        valid = sb("valid", [P, BT, F])
        found = sb("found", [P, BT, F])
        table_start = sb("table_start", [P, BT, F], I32)
        row = sb("row", [P, BT, F], U32)
        tok = sb("tok", [TOK_P, CARD // TOK_P], I32)
        tok_want = sb("tok_want", [TOK_P, CARD // TOK_P], I32)
        tok_bad = sb("tok_bad", [TOK_P, CARD // TOK_P])
        tok_bad_any = sb("tok_bad_any", [TOK_P, 1])
        ones = sb("ones", [P, 1])
        bad_count = sb("bad_count", [1, 1], I32)
        tok_all = sb("tok_all", [P, CHUNK], I32)
        tok_hi = sb("tok_hi", [P, CHUNK], I32)
        tok_lo = sb("tok_lo", [P, CHUNK], I32)
        rank_i = sb("rank_i", [P, CHUNK], I32)
        rank = sb("rank", [P, CHUNK])
        match = sb("match", [P, CHUNK])
        chunk_best = sb("chunk_best", [P, Q])
        best = sb("best", [P, Q])
        dense_in = sb("dense_in", [P, BT, D_DENSE])
        tower_in = sb("tower_in", [P, BT, F + 1, E])
        ident = sb("ident", [P, P])
        w1 = sb("w1", [P, PAIRS, P])
        w2 = sb("w2", [P, PAIRS, P])
        bias1 = sb("bias1", [P, PAIRS])
        bias2 = sb("bias2", [P, 2])
        hidden = sb("hidden", [P, 4, B])
        feat = sb("feat", [P, 2, B])
        staged = sb("staged", [P, 2, B])
        cur = sb("cur", [P, 2, B])
        prod = sb("prod", [P, 2, 2, B])
        x_head = sb("x_head", [P, 2, 2, B], F32R)
        x_tail = sb("x_tail", [P, 2, 2, B], F32R)
        tower_in_t = prod[:, :, :, :].rearrange("p a b n -> p (a b) n")
        w_ij = sb("w_ij", [P, W_RING, 2, N_HID])
        w_ji = sb("w_ji", [P, W_RING, 2, N_HID])
        w_head = sb("w_head", [P, 2, 2, N_HID], F32R)
        w_tail = sb("w_tail", [P, 2, 2, N_HID], F32R)
        head_b1 = sb("head_b1", [P, NT])
        head_w2 = sb("head_w2", [P, NT])
        head_b2 = sb("head_b2", [1, 1])
        result = sb("result", [1, B])

        query_loaded = sem("query_loaded")
        tok_loaded = sem("tok_loaded")
        dense_loaded = sem("dense_loaded")
        w1_loaded = sem("w1_loaded")
        w2_loaded = sem("w2_loaded")
        bias_loaded = sem("bias_loaded")
        head_loaded = sem("head_loaded")
        pool_consts = sem("pool_consts")
        zeroed = sem("zeroed")
        dve_step = sem("dve_step")
        tok_checked = sem("tok_checked")
        bad_summed = sem("bad_summed")
        bad_ready = sem("bad_ready")
        chunk_loaded = sem("chunk_loaded")
        chunk_used = sem("chunk_used")
        gen_step = sem("gen_step")
        rows_ready = sem("rows_ready")
        gathered = [sem(f"gathered_{t}") for t in range(BT)]
        dense_placed = sem("dense_placed")
        transposed = sem("transposed")
        in_t_by_act = sem("in_t_by_act")
        in_t_by_dve = sem("in_t_by_dve")
        layer1_done = sem("layer1_done")
        hidden_by_act = sem("hidden_by_act")
        hidden_by_dve = sem("hidden_by_dve")
        layer2_done = sem("layer2_done")
        feat_ready = sem("feat_ready")
        feat_stored = sem("feat_stored")
        staged_loaded = sem("staged_loaded")
        staged_free = sem("staged_free")
        lower_spread = sem("lower_spread")
        w_loaded = [sem(f"w_loaded_{s}") for s in range(W_RING)]
        w_summed = sem("w_summed")
        prod_ready = sem("prod_ready")
        w_head_ready = sem("w_head_ready")
        x_head_ready = sem("x_head_ready")
        w_tail_ready = sem("w_tail_ready")
        x_tail_ready = sem("x_tail_ready")
        steps_done = sem("steps_done")
        bank_done = sem("bank_done")
        act_hid = sem("act_hid")
        dve_hid = sem("dve_hid")
        logits_done = sem("logits_done")
        result_ready = sem("result_ready")
        result_stored = sem("result_stored")

        W_DMAS = 3 * 16
        ST_DMAS = 3 * 16

        def w_rows(offset, pattern):
            return bass.AP(pw1.tensor, offset * N_HID, [[s * N_HID, n] for s, n in pattern] + [[1, N_HID]])

        def w_step_loads(eng, m, t, slot):
            G = P // m
            for u in range(2):
                eng.dma_start(w_ij[:, slot, u, :], w_rows((t + u) * C + m, [[2 * m * (C + 1), G], [1, m]])
                              ).then_inc(w_loaded[slot], 16)
            ji = bass.AP(pw1.tensor, (m * C + t) * N_HID,
                         [[2 * m * (C + 1) * N_HID, G], [C * N_HID, m], [1, 2 * N_HID]])
            eng.dma_start(w_ji[:, slot].rearrange("p u n -> p (u n)"), ji).then_inc(w_loaded[slot], 16)

        def feat_rows(offset, pattern):
            return bass.AP(c_dram, offset * B, [[s * B, n] for s, n in pattern] + [[1, B]])

        block = ctx.enter_context(nc.Block())

        @block.sync
        def _(sp):
            sp.dma_start(query[:], sparse.rearrange("(p t) f -> p t f", t=BT)).then_inc(query_loaded, 16)
            sp.dma_start(tok[:], tokens.rearrange("(p n) -> p n", p=TOK_P)).then_inc(tok_loaded, 16)
            sp.dma_start(dense_in[:], dense.rearrange("(p t) d -> p t d", t=BT)).then_inc(dense_loaded, 16)
            sp.wait_ge(zeroed, 2)
            sp.dma_start(w1[0:D_DENSE, 0, 0:SLOT], dw1).then_inc(w1_loaded, 16)
            sp.dma_start(w1[SLOT:P, :, SLOT:P], sw1[0:F:2].rearrange("f e h -> e f h")).then_inc(w1_loaded, 16)
            sp.dma_start(w1[0:SLOT, 1:PAIRS, 0:SLOT], sw1[1:F:2].rearrange("f e h -> e f h")).then_inc(w1_loaded, 16)
            for s in range(F + 1):
                at = SLOT * (s % 2)
                sp.dma_start(w2[at:at + SLOT, s // 2, S_OUT * (s % 4):S_OUT * (s % 4 + 1)],
                             dw2 if s == 0 else sw2[s - 1]).then_inc(w2_loaded, 16)
            first = 0
            for m in (128, 64, 32, 16):
                if not first:
                    for slot in range(W_RING):
                        w_step_loads(sp, m, 2 * slot, slot)
                with sp.Fori(0 if first else 1, m // 2 // W_RING) as it:
                    for slot in range(W_RING):
                        sp.wait_ge(w_tail_ready, it * W_RING + (first + slot + 1 - W_RING))
                        w_step_loads(sp, m, it * (2 * W_RING) + 2 * slot, slot)
                first += m // 2
            for m in (8, 4, 2):
                for t in range(0, m, 2):
                    sp.wait_ge(w_tail_ready, first + 1 - W_RING)
                    w_step_loads(sp, m, t, first % W_RING)
                    first += 1
            sp.wait_ge(w_tail_ready, SQUARES + 1 - W_RING)
            for h in range(2):
                sp.dma_start(w_ij[:, SQUARES % W_RING, h, :], w_rows(h * P * (C + 1), [[C + 1, P]])
                             ).then_inc(w_loaded[SQUARES % W_RING], 16)
            sp.wait_ge(w_tail_ready, LAST + 1 - W_RING)
            sp.dma_start(w_ij[:, LAST % W_RING, 0, :], w_rows(1, [[2 * (C + 1), P]])
                         ).then_inc(w_loaded[LAST % W_RING], 16)
            sp.dma_start(w_ji[:, LAST % W_RING, 0, :], w_rows(C, [[2 * (C + 1), P]])
                         ).then_inc(w_loaded[LAST % W_RING], 16)
            sp.wait_ge(result_ready, 1)
            sp.dma_start(out.rearrange("(a n) -> a n", a=1), result[:]).then_inc(result_stored, 16)
            sp.wait_ge(result_stored, 16)

        @block.gpsimd
        def _(pool):
            nc.gpsimd.iota(tok_want[:], [[1, CARD // TOK_P]], base=0, channel_multiplier=CARD // TOK_P
                           ).then_inc(pool_consts, 1)
            nc.gpsimd.iota(table_start[:], [[0, BT], [CARD, F]], base=0, channel_multiplier=0
                           ).then_inc(pool_consts, 1)
            nc.gpsimd.memset(w1[:], 0.0).then_inc(zeroed, 1)
            nc.gpsimd.memset(w2[:], 0.0).then_inc(zeroed, 1)
            nc.gpsimd.iota(rank_i[:], [[-1, CHUNK]], base=CARD, channel_multiplier=0).then_inc(pool_consts, 1)
            nc.gpsimd.memset(ident[:], 0.0).then_inc(pool_consts, 1)
            pool.wait_ge(pool_consts, 4)
            nc.gpsimd.affine_select(out=ident[:], in_=ident[:], compare_op=ALU.not_equal, fill=1.0, base=0,
                                    pattern=[[-1, P]], channel_multiplier=1).then_inc(pool_consts, 1)
            pool.wait_ge(bad_ready, 1)
            bad = pool.value_load(bad_count[0:1, 0:1], min_val=0, max_val=TOK_P)
            with pool.If(bad > 0):
                with pool.Fori(0, N_CHUNKS) as ch:
                    chunk = bass.AP(tokens.tensor, ch * CHUNK, [[0, P], [1, CHUNK]])
                    pool.dma_start(tok_all[:], chunk).then_inc(chunk_loaded, 16)
                    pool.wait_ge(chunk_used, ch + 1)
            emb_rows = emb.rearrange("f c e -> (f c) e")
            pool.wait_ge(rows_ready, 1)
            for t in range(BT):
                for f in range(F):
                    pool.indirect_dma_start(
                        out=tower_in[:, t, f + 1, :], out_offset=None, in_=emb_rows,
                        in_offset=bass.IndirectOffsetOnAxis(ap=row[:, t, f:f + 1], axis=0),
                    ).then_inc(gathered[t], 16)
            pool.wait_ge(feat_stored, 16 * NH)
            for r, (m, k, _n) in enumerate(ROUNDS):
                if r:
                    pool.wait_ge(staged_free, r)
                pool.dma_start(staged[:, 0, :], feat_rows(m, [[2 * m, P // m], [1, m]])
                               ).then_inc(staged_loaded, 16)
                for half in range(2):
                    if m == 128:
                        rows = feat_rows(32 * k, [[0, 2], [1, 32]])
                    elif m == 64:
                        rows = feat_rows(2 * m * half + 32 * k, [[0, 2], [1, 32]])
                    else:
                        rows = feat_rows(P * half, [[2 * m, P // 2 // m], [1, m]])
                    pool.dma_start(staged[64 * half:64 * half + 64, 1, :], rows).then_inc(staged_loaded, 16)

        @block.scalar
        def _(act):
            act.dma_start(bias1[0:SLOT, 0:1], db1.rearrange("(p a) -> p a", a=1)).then_inc(bias_loaded, 16)
            act.dma_start(bias1[SLOT:P, 0:1], sb1[0:1].rearrange("f h -> h f")).then_inc(bias_loaded, 16)
            for p in range(1, PAIRS):
                act.dma_start(bias1[:, p:p + 1], sb1[2 * p - 1:2 * p + 1].rearrange("f (h a) -> (f h) a", a=1)
                              ).then_inc(bias_loaded, 16)
            in_first = P // S_OUT - 1
            act.dma_start(bias2[0:S_OUT, 0:1], db2.rearrange("(p a) -> p a", a=1)).then_inc(bias_loaded, 16)
            act.dma_start(bias2[S_OUT:P, 0:1], sb2[0:in_first].rearrange("f (h a) -> (f h) a", a=1)
                          ).then_inc(bias_loaded, 16)
            act.dma_start(bias2[:, 1:2], sb2[in_first:F].rearrange("f (h a) -> (f h) a", a=1)
                          ).then_inc(bias_loaded, 16)
            with nc.allow_non_contiguous_dma(reason="512 values each"):
                act.dma_start(head_b1[:], pb1.rearrange("(t p) -> p t", p=P)).then_inc(head_loaded, 16)
                act.dma_start(head_w2[:], pw2.rearrange("(t p) a -> p (t a)", p=P)).then_inc(head_loaded, 16)
            act.dma_start(head_b2[:], pb2.rearrange("(p a) -> p a", a=1)).then_inc(head_loaded, 16)

            act.wait_ge(bias_loaded, 16 * (PAIRS + 4))
            for h in range(NH):
                for t in range(h * BT // NH, (h + 1) * BT // NH):
                    if t % 2 == 0:
                        act.wait_ge(transposed, t + 1)
                        nc.scalar.copy(tower_in_t[:, :, t * P:(t + 1) * P],
                                       psum[:, t, :].rearrange("p (a n) -> p a n", a=PAIRS)).then_inc(in_t_by_act, 1)
                for p in range(0, PAIRS, 2):
                    act.wait_ge(layer1_done, h * PAIRS + p + 1)
                    nc.scalar.activation(hidden[:, p, h * HALF:(h + 1) * HALF], psum[:, 4 * h + p, :], ACT.Relu,
                                         bias=bias1[:, p:p + 1]).then_inc(hidden_by_act, 1)
                act.wait_ge(layer2_done, 2 * h + 1)
                nc.scalar.activation(feat[:, 0, h * HALF:(h + 1) * HALF], psum[:, 4 * h, :], ACT.Identity,
                                     bias=bias2[:, 0:1]).then_inc(feat_ready, 1)
                act.wait_ge(feat_ready, 2 * (h + 1))
                act.dma_start(c_dram.ap().rearrange("(c p) n -> p c n", p=P)[:, :, h * HALF:(h + 1) * HALF],
                              feat[:, :, h * HALF:(h + 1) * HALF]).then_inc(feat_stored, 16)

            def split_heads(step, parity, slot, weights, count, tiles=2, reused=True):
                if reused:
                    act.wait_ge(steps_done, step - 1)
                act.wait_ge(weights, count)
                nc.scalar.copy(w_head[:, parity, 0:tiles, :], w_ij[:, slot, 0:tiles, :]).then_inc(w_head_ready, 1)
                act.wait_ge(prod_ready, step + 1)
                nc.scalar.copy(x_head[:, parity, 0:tiles, :], prod[:, parity, 0:tiles, :]).then_inc(x_head_ready, 1)

            for step in range(W_RING):
                split_heads(step, step % 2, step, w_summed, step + 1, reused=step >= 2)
            with act.Fori(1, SQUARES // W_RING) as it:
                for slot in range(W_RING):
                    split_heads(it * W_RING + slot, slot % 2, slot, w_summed, it * W_RING + slot + 1)
            for step in range(SQUARES // W_RING * W_RING, SQUARES):
                split_heads(step, step % 2, step % W_RING, w_summed, step + 1)
            split_heads(SQUARES, SQUARES % 2, SQUARES % W_RING, w_loaded[SQUARES % W_RING],
                        SQUARES // W_RING * W_DMAS + 2 * 16)
            split_heads(LAST, LAST % 2, LAST % W_RING, w_summed, LAST, tiles=1)

            act.wait_ge(head_loaded, 48)
            for bank in range(0, 8, 2):
                act.wait_ge(bank_done, bank + 1)
                nc.scalar.activation(hidden[:, bank // NH, (bank % NH) * HALF:(bank % NH + 1) * HALF],
                                     psum[:, bank, :], ACT.Relu, bias=head_b1[:, bank // NH:bank // NH + 1]
                                     ).then_inc(act_hid, 1)
            for h in range(NH):
                act.wait_ge(logits_done, h + 1)
                half_tiles = HALF // P
                nc.scalar.activation(
                    result[0:1, :].rearrange("a (p t) -> a t p", t=BT)[:, h * half_tiles:(h + 1) * half_tiles, :],
                    psum[0:1, h, :].rearrange("a (t p) -> a t p", p=P), ACT.Sigmoid, bias=head_b2[0:1, 0:1]
                ).then_inc(result_ready if h == NH - 1 else act_hid, 1)

        @block.vector
        def _(dve):
            chain = [0]

            def link(ins):
                chain[0] += 1
                ins.then_inc(dve_step, 1)
                dve.wait_ge(dve_step, chain[0])

            v = nc.vector
            v.memset(ones[:], 1.0)
            link(v.memset(tower_in[:, :, 0, :], 0.0))
            dve.wait_ge(tok_loaded, 16)
            dve.wait_ge(pool_consts, 1)
            link(v.tensor_tensor(tok_bad[:], tok[:], tok_want[:], ALU.not_equal))
            v.reduce_max(tok_bad_any[:], tok_bad[:], AX_X).then_inc(tok_checked, 1)
            dve.wait_ge(query_loaded, 16)
            link(v.tensor_scalar(valid[:], query[:], 0.0, None, ALU.is_ge))
            link(v.scalar_tensor_tensor(out=valid[:], in0=query[:], scalar=float(CARD - 1), in1=valid[:],
                                        op0=ALU.is_le, op1=ALU.mult))
            link(v.tensor_tensor(found[:], query[:], valid[:], ALU.mult))
            dve.wait_ge(bad_summed, 1)
            v.tensor_copy(bad_count[:], psum[0:1, 0, 0:1]).then_inc(bad_ready, 1)
            dve.wait_ge(bad_ready, 1)
            bad = dve.value_load(bad_count[0:1, 0:1], min_val=0, max_val=TOK_P)
            with dve.If(bad > 0):
                gen = [0]

                def glink(ins):
                    gen[0] += 1
                    ins.then_inc(gen_step, 1)
                    dve.wait_ge(gen_step, gen[0])

                dve.wait_ge(pool_consts, 3)
                glink(v.tensor_single_scalar(query_hi[:], query[:], 16, ALU.arith_shift_right))
                glink(v.tensor_single_scalar(query_lo[:], query[:], 0xFFFF, ALU.bitwise_and))
                glink(v.tensor_copy(query_hi_f[:], query_hi[:]))
                glink(v.tensor_copy(query_lo_f[:], query_lo[:]))
                glink(v.tensor_copy(rank[:], rank_i[:]))
                glink(v.memset(best[:], 0.0))
                before, per_chunk = gen[0], 2 + 3 * Q + 2
                hi_f = query_hi_f[:].rearrange("p t f -> p (t f)")
                lo_f = query_lo_f[:].rearrange("p t f -> p (t f)")
                with dve.Fori(0, N_CHUNKS) as ch:
                    inner = [0]

                    def clink(ins):
                        inner[0] += 1
                        ins.then_inc(gen_step, 1)
                        dve.wait_ge(gen_step, ch * per_chunk + (before + inner[0]))

                    dve.wait_ge(chunk_loaded, ch * 16 + 16)
                    clink(v.tensor_single_scalar(tok_hi[:], tok_all[:], 16, ALU.arith_shift_right))
                    clink(v.tensor_single_scalar(tok_lo[:], tok_all[:], 0xFFFF, ALU.bitwise_and))
                    for q in range(Q):
                        clink(v.scalar_tensor_tensor(out=match[:], in0=tok_lo[:], scalar=lo_f[:, q:q + 1],
                                                     in1=rank[:], op0=ALU.is_equal, op1=ALU.mult))
                        clink(v.scalar_tensor_tensor(out=match[:], in0=tok_hi[:], scalar=hi_f[:, q:q + 1],
                                                     in1=match[:], op0=ALU.is_equal, op1=ALU.mult))
                        clink(v.reduce_max(chunk_best[:, q:q + 1], match[:], AX_X))
                    clink(v.tensor_tensor(best[:], best[:], chunk_best[:], ALU.max))
                    clink(v.tensor_scalar(rank[:], rank[:], -float(CHUNK), None, ALU.add))
                    assert inner[0] == per_chunk
                    dve.sem_inc(chunk_used, 1)
                end = before + per_chunk * N_CHUNKS
                best3 = best[:].rearrange("p (t f) -> p t f", f=F)
                for n, ins in enumerate((
                    lambda: v.tensor_scalar(valid[:], best3, 0.0, None, ALU.is_gt),
                    lambda: v.tensor_scalar(found[:], best3, -1.0, float(CARD), ALU.mult, ALU.add),
                    lambda: v.tensor_tensor(found[:], found[:], valid[:], ALU.mult),
                )):
                    ins().then_inc(gen_step, 1)
                    dve.wait_ge(gen_step, end + n + 1)
            dve.wait_ge(pool_consts, 2)
            v.tensor_tensor(row[:], found[:], table_start[:], ALU.add).then_inc(rows_ready, 1)
            dve.wait_ge(dense_loaded, 16)
            v.tensor_copy(tower_in[:, :, 0, 0:D_DENSE], dense_in[:]).then_inc(dense_placed, 1)

            dve.wait_ge(bias_loaded, 16 * (PAIRS + 4))
            for h in range(NH):
                for t in range(h * BT // NH, (h + 1) * BT // NH):
                    if t % 2 == 1:
                        dve.wait_ge(transposed, t + 1)
                        v.tensor_copy(tower_in_t[:, :, t * P:(t + 1) * P],
                                      psum[:, t, :].rearrange("p (a n) -> p a n", a=PAIRS)).then_inc(in_t_by_dve, 1)
                for p in range(1, PAIRS, 2):
                    dve.wait_ge(layer1_done, h * PAIRS + p + 1)
                    v.tensor_scalar(hidden[:, p, h * HALF:(h + 1) * HALF], psum[:, 4 * h + p, :], bias1[:, p:p + 1],
                                    0.0, ALU.add, ALU.max).then_inc(hidden_by_dve, 1)
                dve.wait_ge(layer2_done, 2 * h + 2)
                v.tensor_scalar(feat[:, 1, h * HALF:(h + 1) * HALF], psum[:, 4 * h + 1, :], bias2[:, 1:2], None,
                                ALU.add).then_inc(feat_ready, 1)

            def start_round(r):
                dve.wait_ge(staged_loaded, r * ST_DMAS + ST_DMAS)
                v.tensor_copy(cur[:].rearrange("p a n -> p (a n)"), staged[:].rearrange("p a n -> p (a n)")
                              ).then_inc(staged_free, 1)
                dve.wait_ge(staged_free, r + 1)

            def sum_weights(slot, use):
                flat = "p u n -> p (u n)"
                dve.wait_ge(w_loaded[slot], use * W_DMAS + W_DMAS)
                v.tensor_tensor(w_ij[:, slot].rearrange(flat), w_ij[:, slot].rearrange(flat),
                                w_ji[:, slot].rearrange(flat), ALU.add).then_inc(w_summed, 1)

            def spread_lower(m, t, parity):
                for u in range(2):
                    mask = [lane // m * m + t + u if m < 32 else t + u for lane in range(32)]
                    ins = v.stream_shuffle(prod[:, parity, u, :], cur[:, 1, :], mask)
                ins.then_inc(lower_spread, 1)

            def multiply(step, parity):
                dve.wait_ge(lower_spread, step + 1)
                v.tensor_tensor(prod[:, parity], prod[:, parity],
                                cur[:, 0:1, :].to_broadcast([P, 2, B]), ALU.mult).then_inc(prod_ready, 1)

            def weight_tails(step, parity, slot, tiles=2):
                dve.wait_ge(w_head_ready, step + 1)
                v.tensor_tensor(w_tail[:, parity, 0:tiles, :], w_ij[:, slot, 0:tiles, :],
                                w_head[:, parity, 0:tiles, :].bitcast(F32), ALU.subtract).then_inc(w_tail_ready, 1)

            def product_tails(step, parity, tiles=2):
                dve.wait_ge(x_head_ready, step + 1)
                v.tensor_tensor(x_tail[:, parity, 0:tiles, :], prod[:, parity, 0:tiles, :],
                                x_head[:, parity, 0:tiles, :].bitcast(F32), ALU.subtract).then_inc(x_tail_ready, 1)

            with dve.Fori(0, len(LOOPED)) as r:
                start_round(r)
                for s in range(PER_ROUND):
                    step = r * PER_ROUND + s
                    sum_weights(s % W_RING, r * (PER_ROUND // W_RING) + s // W_RING)
                    if s:
                        if s >= 2:
                            dve.wait_ge(x_tail_ready, r * PER_ROUND + (s - 1))
                        weight_tails(r * PER_ROUND + (s - 1), (s - 1) % 2, (s - 1) % W_RING)
                    spread_lower(32, 2 * s, s % 2)
                    if s:
                        product_tails(r * PER_ROUND + (s - 1), (s - 1) % 2)
                    multiply(step, s % 2)
                weight_tails(r * PER_ROUND + (PER_ROUND - 1), 1, W_RING - 1)
                product_tails(r * PER_ROUND + (PER_ROUND - 1), 1)
                dve.wait_ge(prod_ready, r * PER_ROUND + PER_ROUND)
                dve.wait_ge(x_tail_ready, r * PER_ROUND + PER_ROUND)
            step = TAIL_AT
            for number, (m, _k, n) in enumerate(TAIL[:-1], len(LOOPED)):
                dve.wait_ge(prod_ready, step)
                start_round(number)
                for s in range(n):
                    sum_weights(step % W_RING, step // W_RING)
                    if step > TAIL_AT:
                        weight_tails(step - 1, (step - 1) % 2, (step - 1) % W_RING)
                    dve.wait_ge(x_tail_ready, step - 1)
                    spread_lower(m, 2 * s, step % 2)
                    if step > TAIL_AT:
                        product_tails(step - 1, (step - 1) % 2)
                    multiply(step, step % 2)
                    step += 1
            dve.wait_ge(x_tail_ready, SQUARES - 1)
            v.tensor_tensor(prod[:, SQUARES % 2], feat[:], feat[:], ALU.mult).then_inc(prod_ready, 1)
            weight_tails(SQUARES - 1, (SQUARES - 1) % 2, (SQUARES - 1) % W_RING)
            product_tails(SQUARES - 1, (SQUARES - 1) % 2)
            dve.wait_ge(prod_ready, LAST)
            start_round(len(ROUNDS) - 1)
            dve.wait_ge(w_loaded[LAST % W_RING], LAST // W_RING * W_DMAS + 2 * 16)
            v.tensor_tensor(w_ij[:, LAST % W_RING, 0, :], w_ij[:, LAST % W_RING, 0, :],
                            w_ji[:, LAST % W_RING, 0, :], ALU.add).then_inc(w_summed, 1)
            dve.wait_ge(x_tail_ready, LAST - 1)
            v.tensor_tensor(prod[:, LAST % 2, 0, :], cur[:, 0, :], cur[:, 1, :], ALU.mult).then_inc(prod_ready, 1)
            weight_tails(SQUARES, SQUARES % 2, SQUARES % W_RING)
            product_tails(SQUARES, SQUARES % 2)
            weight_tails(LAST, LAST % 2, LAST % W_RING, tiles=1)
            product_tails(LAST, LAST % 2, tiles=1)

            dve.wait_ge(head_loaded, 48)
            for bank in range(1, 8, 2):
                dve.wait_ge(bank_done, bank + 1)
                v.tensor_scalar(hidden[:, bank // NH, (bank % NH) * HALF:(bank % NH + 1) * HALF], psum[:, bank, :],
                                head_b1[:, bank // NH:bank // NH + 1], 0.0, ALU.add, ALU.max).then_inc(dve_hid, 1)

        @block.tensor
        def _(pe):
            pe.wait_ge(tok_checked, 1)
            pe.matmul(psum[0:1, 0, 0:1], tok_bad_any[:], ones[0:TOK_P, :], start=True, stop=True
                      ).then_inc(bad_summed, 1)
            pe.wait_ge(pool_consts, 5)
            pe.wait_ge(bad_ready, 1)
            pe.wait_ge(dense_placed, 1)
            pe.wait_ge(w1_loaded, 3 * 16)
            pe.wait_ge(w2_loaded, (F + 1) * 16)
            per_half = BT // NH
            for h in range(NH):
                for t in range(h * per_half, (h + 1) * per_half):
                    pe.wait_ge(gathered[t], F * 16)
                    for p in range(PAIRS):
                        ins = pe.transpose(psum[:, t, p * P:(p + 1) * P],
                                           tower_in[:, t, 2 * p:2 * p + 2, :].rearrange("p s e -> p (s e)"), ident[:])
                    ins.then_inc(transposed, 1)
                pe.wait_ge(in_t_by_act, (h + 1) * per_half // 2)
                pe.wait_ge(in_t_by_dve, (h + 1) * per_half // 2)
                for p in range(PAIRS):
                    pe.matmul(psum[:, 4 * h + p, :], w1[:, p, :], tower_in_t[:, p, h * HALF:(h + 1) * HALF],
                              start=True, stop=True).then_inc(layer1_done, 1)
                pe.wait_ge(hidden_by_act, (h + 1) * PAIRS // 2)
                pe.wait_ge(hidden_by_dve, (h + 1) * PAIRS // 2)
                for c in range(2):
                    for p in (2 * c, 2 * c + 1):
                        ins = pe.matmul(psum[:, 4 * h + c, :], w2[:, p, :], hidden[:, p, h * HALF:(h + 1) * HALF],
                                        start=(p == 2 * c), stop=(p == 2 * c + 1))
                    ins.then_inc(layer2_done, 1)
            pe.wait_ge(feat_ready, 2 * NH)

            def banks():
                return [(b, b // NH, b % NH) for b in range(8)]

            def k_tile(parity, u, first=False, last=False):
                for b, nt, h in banks():
                    units = slice(nt * P, (nt + 1) * P)
                    cols = slice(h * HALF, (h + 1) * HALF)
                    terms = ((w_head, x_head), (w_tail, x_head), (w_head, x_tail))
                    for n, (w, x) in enumerate(terms):
                        ins = pe.matmul(psum[:, b, :], w[:, parity, u, units], x[:, parity, u, cols],
                                        start=first and n == 0, stop=last and n == 2)
                    if last:
                        ins.then_inc(bank_done, 1)
                return ins

            def step_products(step, parity, first=False):
                pe.wait_ge(w_tail_ready, step + 1)
                pe.wait_ge(x_tail_ready, step + 1)
                k_tile(parity, 0, first=first)
                k_tile(parity, 1).then_inc(steps_done, 1)

            step_products(0, 0, first=True)
            step_products(1, 1)
            with pe.Fori(1, LAST // 2) as it:
                for parity in range(2):
                    step_products(it * 2 + parity, parity)
            pe.wait_ge(w_tail_ready, LAST + 1)
            pe.wait_ge(x_tail_ready, LAST + 1)
            k_tile(LAST % 2, 0, last=True)

            pe.wait_ge(act_hid, 4)
            pe.wait_ge(dve_hid, 4)
            for h in range(NH):
                for nt in range(NT):
                    ins = pe.matmul(psum[0:1, h, :], head_w2[:, nt:nt + 1], hidden[:, nt, h * HALF:(h + 1) * HALF],
                                    start=(nt == 0), stop=(nt == NT - 1))
                ins.then_inc(logits_done, 1)


_INS = ["r_dense_features", "r_sparse_features", "L0_rec_tokenizers", "L0_rec_emb_tables", "L0_rec_dw1",
        "L0_rec_db1", "L0_rec_dw2", "L0_rec_db2", "L0_rec_sw1", "L0_rec_sb1", "L0_rec_sw2", "L0_rec_sb2",
        "L0_rec_pw1", "L0_rec_pb1", "L0_rec_pw2", "L0_rec_pb2"]


def kernel(**inputs):
    import numpy as np
    import concourse.bacc as bacc
    from concourse.bass_utils import run_bass_kernel_spmd

    nc = bacc.Bacc("TRN2", target_bir_lowering=False, num_devices=1)
    arrays, args = {}, []
    for name in _INS:
        a = np.ascontiguousarray(inputs[name])
        arrays[f"in_{name}"] = a
        args.append(nc.dram_tensor(f"in_{name}", a.shape, mybir.dt.from_np(a.dtype), kind="ExternalInput").ap())
    out = nc.dram_tensor("out_probability", (arrays["in_r_dense_features"].shape[0],), F32, kind="ExternalOutput").ap()
    rec_kernel(nc, *args, out)
    r = run_bass_kernel_spmd(nc, [arrays], core_ids=[0])
    return r.results[0]["out_probability"]
```

```python
from contextlib import ExitStack

import concourse.bass as bass
from concourse import mybir

ALU = mybir.AluOpType
ACT = mybir.ActivationFunctionType
AX_X = mybir.AxisListType.X
F32 = mybir.dt.float32
F32R = mybir.dt.float32r
I32 = mybir.dt.int32
U32 = mybir.dt.uint32
P = 128


def rec_kernel(nc, dense, sparse, tokens, emb, dw1, db1, dw2, db2, sw1, sb1, sw2, sb2, pw1, pb1, pw2, pb2, out):
    B, D_DENSE = dense.shape
    F, CARD, E = emb.shape
    S_OUT = sw2.shape[2]
    C = (F + 1) * S_OUT
    N_HID = pw1.shape[1]
    BT = B // P
    HALF = 512
    NH = B // HALF
    NT = N_HID // P
    PAIRS = (F + 1) // 2
    SLOT = E
    assert E == sw1.shape[2] == dw1.shape[1] and 2 * E == P and C == 2 * P and dw2.shape[1] == S_OUT
    assert NT * NH == 8 and BT * P == B

    BLOCK, GROUP = "block", "group"
    N_BLOCKS = C // 64
    ROUNDS = ([((BLOCK, 32), z, 4) for z in range(N_BLOCKS)]
              + [((GROUP, 64), k, 8) for k in range(4)]
              + [((GROUP, 128), k, 16) for k in range(4)])
    TAIL = [((GROUP, m), 0, m // 2) for m in (16, 8, 4, 2)] + [((GROUP, 1), 0, 2)]
    BLOCK_STEPS = 4
    TAIL_ROUND = len(ROUNDS)
    FIRST_64, FIRST_128, FIRST_TAIL = (sum(n for _, _, n in ROUNDS[:k]) for k in (N_BLOCKS, N_BLOCKS + 4, TAIL_ROUND))
    ROUNDS = ROUNDS + TAIL
    STEPS = sum(n for _, _, n in ROUNDS)
    SQUARES, LAST = STEPS - 2, STEPS - 1
    PARK_AFTER = BLOCK_STEPS
    N_EARLY = 2
    W_RING = 4
    CHUNK = 1000
    N_CHUNKS = CARD // CHUNK
    TOK_P = 80
    Q = BT * F
    assert CARD % CHUNK == 0 and CARD % TOK_P == 0 and STEPS == 129

    with ExitStack() as ctx:
        def sb(name, shape, dt=F32):
            return ctx.enter_context(nc.sbuf_tensor(name, shape, dt))

        def sem(name):
            return ctx.enter_context(nc.semaphore(name))

        c_dram = nc.dram_tensor("features_dram", (C, B), F32, kind="Internal")

        psum = ctx.enter_context(nc.psum_tensor("psum", [P, 8, HALF], F32))
        query = sb("query", [P, BT, F], I32)
        query_hi = sb("query_hi", [P, BT, F], I32)
        query_lo = sb("query_lo", [P, BT, F], I32)
        query_hi_f = sb("query_hi_f", [P, BT, F])
        query_lo_f = sb("query_lo_f", [P, BT, F])
        valid = sb("valid", [P, BT, F])
        found = sb("found", [P, BT, F])
        table_start = sb("table_start", [P, BT, F], I32)
        row = sb("row", [P, BT, F], U32)
        tok = sb("tok", [TOK_P, CARD // TOK_P], I32)
        tok_want = sb("tok_want", [TOK_P, CARD // TOK_P], I32)
        tok_bad = sb("tok_bad", [TOK_P, CARD // TOK_P])
        tok_bad_any = sb("tok_bad_any", [TOK_P, 1])
        ones = sb("ones", [P, 1])
        bad_count = sb("bad_count", [1, 1], I32)
        tok_all = sb("tok_all", [P, CHUNK], I32)
        rank_i = sb("rank_i", [P, CHUNK], I32)
        chunk_best = sb("chunk_best", [P, Q])
        best = sb("best", [P, Q])
        dense_in = sb("dense_in", [P, BT, D_DENSE])
        tower_in = sb("tower_in", [P, BT, F + 1, E])
        ident = sb("ident", [P, P])
        w1 = sb("w1", [P, PAIRS, P])
        w2 = sb("w2", [P, PAIRS, 2 * S_OUT])
        w2_lane = sb("w2_lane", [P, 2, P])
        bias1 = sb("bias1", [P, PAIRS])
        bias2 = sb("bias2", [2 * S_OUT, PAIRS])
        bias_lane = sb("bias_lane", [P, 2])
        tower_in_t = sb("tower_in_t", [P, PAIRS, B])
        hidden = sb("hidden", [P, 4, B])
        tok_hi = hidden[:, 0, 0:CHUNK].bitcast(I32)
        tok_lo = hidden[:, 1, 0:CHUNK].bitcast(I32)
        rank = hidden[:, 2, 0:CHUNK]
        match = hidden[:, 3, 0:CHUNK]
        feat = sb("feat", [P, 2, B])
        staged = sb("staged", [P, 2, B])
        cur = sb("cur", [P, 2, B])
        prod = sb("prod", [P, 2, 2, B])
        x_head = sb("x_head", [P, 2, 2, B], F32R)
        x_tail = sb("x_tail", [P, 2, 2, B], F32R)
        w_ij = sb("w_ij", [P, W_RING, 2, N_HID])
        w_ji = sb("w_ji", [P, W_RING, 2, N_HID])
        w_head = sb("w_head", [P, 2, 2, N_HID], F32R)
        w_tail = sb("w_tail", [P, 2, 2, N_HID], F32R)
        head_b1 = sb("head_b1", [P, NT])
        head_w2 = sb("head_w2", [P, NT])
        head_b2 = sb("head_b2", [1, 1])
        parked = sb("parked", [P, 4, HALF])
        summed = tower_in_t[:, 0:2, :].rearrange("p a (b n) -> p (a b) n", n=HALF)
        score = tower_in_t[:, 2, :].rearrange("p (h n) -> p h n", n=HALF)
        result = sb("result", [1, B])
        sigmoid_warm = sb("sigmoid_warm", [1, 1])

        query_loaded = sem("query_loaded")
        tok_loaded = sem("tok_loaded")
        dense_loaded = sem("dense_loaded")
        w1_loaded = sem("w1_loaded")
        w2_loaded = sem("w2_loaded")
        bias_loaded = sem("bias_loaded")
        head_loaded = sem("head_loaded")
        pool_consts = sem("pool_consts")
        zeroed = sem("zeroed")
        dve_step = sem("dve_step")
        tok_checked = sem("tok_checked")
        bad_summed = sem("bad_summed")
        bad_ready = sem("bad_ready")
        chunk_loaded = sem("chunk_loaded")
        chunk_used = sem("chunk_used")
        gen_step = sem("gen_step")
        rows_ready = sem("rows_ready")
        gathered = [sem(f"gathered_{p}") for p in range(PAIRS)]
        dense_placed = sem("dense_placed")
        ones_ready = sem("ones_ready")
        transposed = sem("transposed")
        in_t_ready = [sem(f"in_t_ready_{h}") for h in range(NH)]
        layer1_done = sem("layer1_done")
        hidden_ready = [sem(f"hidden_ready_{h}") for h in range(NH)]
        layer2_done = sem("layer2_done")
        feat_ready = [sem(f"feat_ready_{h}") for h in range(NH)]
        w2_lane_ready = sem("w2_lane_ready")
        seed_done = sem("seed_done")
        seeded = sem("seeded")
        feat_stored = [sem(f"feat_stored_{p}") for p in range(PAIRS)]
        staged_loaded = sem("staged_loaded")
        staged_free = sem("staged_free")
        lower_spread = sem("lower_spread")
        w_loaded = [sem(f"w_loaded_{s}") for s in range(W_RING)]
        w_summed = sem("w_summed")
        prod_ready = sem("prod_ready")
        w_head_ready = sem("w_head_ready")
        x_head_ready = sem("x_head_ready")
        w_tail_ready = sem("w_tail_ready")
        x_tail_ready = sem("x_tail_ready")
        steps_done = sem("steps_done")
        bank_done = sem("bank_done")
        bank_closed = sem("bank_closed")
        bank_parked = sem("bank_parked")
        bank_summed = sem("bank_summed")
        bank_relu = sem("bank_relu")
        score_step = sem("score_step")
        logits_done = sem("logits_done")
        result_ready = sem("result_ready")
        result_stored = sem("result_stored")

        W_DMAS = 3 * 16
        ST_DMAS = 5 * 16

        def lanes(kind, upper, lower):
            how, m = kind
            if how == BLOCK:
                return [[upper, 32], [8 * lower, 4]]
            by_group = [2 * m * (upper + lower), P // m]
            return [[upper, m], by_group] if m >= 64 else [by_group, [upper, m]]

        def w_step_loads(eng, kind, start, t, slot, tiles=2):
            m = kind[1]
            origin = start * (C + 1)
            for u in range(tiles):
                ij = bass.AP(pw1.tensor, (origin + (t + u) * C + m) * N_HID,
                             [[s * N_HID, n] for s, n in lanes(kind, 1, C)] + [[1, N_HID]])
                eng.dma_start(w_ij[:, slot, u, :], ij).then_inc(w_loaded[slot], 16)
            ji = bass.AP(pw1.tensor, (origin + m * C + t) * N_HID,
                         [[s * N_HID, n] for s, n in lanes(kind, C, 1)] + [[1, tiles * N_HID]])
            eng.dma_start(w_ji[:, slot, 0:tiles, :].rearrange("p u n -> p (u n)"), ji).then_inc(w_loaded[slot], 16)

        def feat_rows(offset, pattern):
            return bass.AP(c_dram, offset * B, [[s * B, n] for s, n in pattern] + [[1, B]])

        def stage_round(eng, kind, k, number):
            how, m = kind
            start = k * 64 if how == BLOCK else 0
            if not (isinstance(number, int) and number == 1):
                eng.wait_ge(staged_free, number - 1)
            eng.dma_start(staged[:, 0, :], feat_rows(start + m, lanes(kind, 1, 0))).then_inc(staged_loaded, 16)
            for q in range(4):
                if how == BLOCK:
                    lower = feat_rows(start, [[1, 32]])
                elif m == 128:
                    lower = feat_rows(k * 32, [[1, 32]])
                elif m == 64:
                    lower = feat_rows(k * 16, [[1, 16], [128, 2]])
                else:
                    lower = feat_rows(64 * q, [[2 * m, 32 // m], [1, m]])
                eng.dma_start(staged[32 * q:32 * q + 32, 1, :], lower).then_inc(staged_loaded, 16)

        def spread_mask(kind, t):
            how, m = kind
            if how == BLOCK:
                return [8 * (lane % 4) + t for lane in range(32)]
            if m == 128:
                return [t] * 32
            if m == 64:
                return [2 * t + lane % 2 for lane in range(32)]
            return [lane // m * m + t for lane in range(32)]

        BIAS_DMAS = 8
        END_ORDER = [4, 5, 6, 7, 0, 1, 2, 3]
        SEED_BANK = 4

        def cols(h):
            return slice(h * HALF, (h + 1) * HALF)

        def block_lanes(p):
            return slice(64 * (p % 2), 64 * (p % 2) + 64)

        def tower_bank(p, h):
            return 2 * p + h

        block = ctx.enter_context(nc.Block())

        @block.sync
        def _(sp):
            sp.dma_start(query[:], sparse.rearrange("(p t) f -> p t f", t=BT)).then_inc(query_loaded, 16)
            sp.dma_start(tok[:], tokens.rearrange("(p n) -> p n", p=TOK_P)).then_inc(tok_loaded, 16)
            sp.dma_start(dense_in[:], dense.rearrange("(p t) d -> p t d", t=BT)).then_inc(dense_loaded, 16)
            sp.wait_ge(zeroed, 2)
            sp.dma_start(w1[0:D_DENSE, 0, 0:SLOT], dw1).then_inc(w1_loaded, 16)
            sp.dma_start(w1[SLOT:P, :, SLOT:P], sw1[0:F:2].rearrange("f e h -> e f h")).then_inc(w1_loaded, 16)
            sp.dma_start(w1[0:SLOT, 1:PAIRS, 0:SLOT], sw1[1:F:2].rearrange("f e h -> e f h")).then_inc(w1_loaded, 16)
            for s in range(F + 1):
                at = SLOT * (s % 2)
                sp.dma_start(w2[at:at + SLOT, s // 2, S_OUT * (s % 2):S_OUT * (s % 2 + 1)],
                             dw2 if s == 0 else sw2[s - 1]).then_inc(w2_loaded, 16)
            for slot in range(BLOCK_STEPS):
                w_step_loads(sp, (BLOCK, 32), 0, 2 * slot, slot)
            with nc.allow_non_contiguous_dma(reason="512 values each"):
                sp.dma_start(head_b1[:], pb1.rearrange("(t p) -> p t", p=P)).then_inc(head_loaded, 16)
                sp.dma_start(head_w2[:], pw2.rearrange("(t p) a -> p (t a)", p=P)).then_inc(head_loaded, 16)
            sp.dma_start(head_b2[:], pb2.rearrange("(p a) -> p a", a=1)).then_inc(head_loaded, 16)
            for z in range(1, N_BLOCKS):
                for slot in range(BLOCK_STEPS):
                    sp.wait_ge(w_tail_ready, z * BLOCK_STEPS + slot + 1 - W_RING)
                    w_step_loads(sp, (BLOCK, 32), z * 64, 2 * slot, slot)
                    if slot == 0:
                        sp.wait_ge(feat_stored[z], 16)
                        if z == N_BLOCKS - 1:
                            sp.wait_ge(feat_stored[0], 16)
                        stage_round(sp, (BLOCK, 32), z, z)
            for m, n, first, before in ((64, 8, FIRST_64, N_BLOCKS), (128, 16, FIRST_128, N_BLOCKS + 4)):
                with sp.Fori(0, 4) as k:
                    for s in range(n):
                        sp.wait_ge(w_tail_ready, k * n + (first + s + 1 - W_RING))
                        w_step_loads(sp, (GROUP, m), 0, k * (2 * n) + 2 * s, s % W_RING)
                        if s == 0:
                            stage_round(sp, (GROUP, m), k, k + before)
            step = FIRST_TAIL
            for number, (kind, _k, n) in enumerate(TAIL[:-1], TAIL_ROUND):
                for s in range(n):
                    sp.wait_ge(w_tail_ready, step + 1 - W_RING)
                    w_step_loads(sp, kind, 0, 2 * s, step % W_RING)
                    if s == 0:
                        stage_round(sp, kind, 0, number)
                    step += 1
            sp.wait_ge(w_tail_ready, SQUARES + 1 - W_RING)
            for h in range(2):
                jj = bass.AP(pw1.tensor, h * P * (C + 1) * N_HID, [[(C + 1) * N_HID, P], [1, N_HID]])
                sp.dma_start(w_ij[:, SQUARES % W_RING, h, :], jj).then_inc(w_loaded[SQUARES % W_RING], 16)
            sp.wait_ge(w_tail_ready, LAST + 1 - W_RING)
            w_step_loads(sp, (GROUP, 1), 0, 0, LAST % W_RING, tiles=1)
            stage_round(sp, (GROUP, 1), 0, len(ROUNDS) - 1)
            sp.wait_ge(result_ready, NH)
            sp.dma_start(out.rearrange("(a n) -> a n", a=1), result[:]).then_inc(result_stored, 16)
            sp.wait_ge(result_stored, 16)

        @block.gpsimd
        def _(pool):
            nc.gpsimd.iota(tok_want[:], [[1, CARD // TOK_P]], base=0, channel_multiplier=CARD // TOK_P
                           ).then_inc(pool_consts, 1)
            nc.gpsimd.iota(table_start[:], [[0, BT], [CARD, F]], base=0, channel_multiplier=0
                           ).then_inc(pool_consts, 1)
            nc.gpsimd.memset(w1[:], 0.0).then_inc(zeroed, 1)
            nc.gpsimd.memset(w2[:], 0.0).then_inc(zeroed, 1)
            nc.gpsimd.iota(rank_i[:], [[-1, CHUNK]], base=CARD, channel_multiplier=0).then_inc(pool_consts, 1)
            nc.gpsimd.memset(ident[:], 0.0).then_inc(pool_consts, 1)
            pool.wait_ge(pool_consts, 4)
            nc.gpsimd.affine_select(out=ident[:], in_=ident[:], compare_op=ALU.not_equal, fill=1.0, base=0,
                                    pattern=[[-1, P]], channel_multiplier=1).then_inc(pool_consts, 1)
            pool.wait_ge(bad_ready, 1)
            bad = pool.value_load(bad_count[0:1, 0:1], min_val=0, max_val=TOK_P)
            with pool.If(bad > 0):
                with pool.Fori(0, N_CHUNKS) as ch:
                    chunk = bass.AP(tokens.tensor, ch * CHUNK, [[0, P], [1, CHUNK]])
                    pool.dma_start(tok_all[:], chunk).then_inc(chunk_loaded, 16)
                    pool.wait_ge(chunk_used, ch + 1)
            emb_rows = emb.rearrange("f c e -> (f c) e")
            pool.wait_ge(rows_ready, 1)
            for f in range(F):
                for t in range(BT):
                    pool.indirect_dma_start(
                        out=tower_in[:, t, f + 1, :], out_offset=None, in_=emb_rows,
                        in_offset=bass.IndirectOffsetOnAxis(ap=row[:, t, f:f + 1], axis=0),
                    ).then_inc(gathered[(f + 1) // 2], 16)

        @block.scalar
        def _(act):
            act.wait_ge(ones_ready, 1)
            nc.scalar.activation(sigmoid_warm[:], ones[0:1, :], ACT.Sigmoid)
            with nc.allow_non_contiguous_dma(reason="a few hundred values"):
                act.dma_start(bias1[0:SLOT, 0:1], db1.rearrange("(p a) -> p a", a=1)).then_inc(bias_loaded, 16)
                act.dma_start(bias1[SLOT:P, 0:1], sb1[0:1].rearrange("f h -> h f")).then_inc(bias_loaded, 16)
                act.dma_start(bias1[:, 1:PAIRS], bass.AP(sb1.tensor, SLOT, [[1, P], [P, PAIRS - 1]])
                              ).then_inc(bias_loaded, 16)
                act.dma_start(bias2[0:S_OUT, 0:1], db2.rearrange("(p a) -> p a", a=1)).then_inc(bias_loaded, 16)
                act.dma_start(bias2[S_OUT:2 * S_OUT, 0:1], sb2[0:1].rearrange("f h -> h f")).then_inc(bias_loaded, 16)
                act.dma_start(bias2[:, 1:PAIRS], bass.AP(sb2.tensor, S_OUT, [[1, 2 * S_OUT], [2 * S_OUT, PAIRS - 1]])
                              ).then_inc(bias_loaded, 16)
                act.dma_start(bias_lane[:, 0:1], bass.AP(sb2.tensor, 0, [[1, S_OUT], [0, P // S_OUT], [1, 1]])
                              ).then_inc(bias_loaded, 16)
                act.dma_start(bias_lane[:, 1:2], bass.AP(db2.tensor, 0, [[0, P // S_OUT], [1, S_OUT], [1, 1]])
                              ).then_inc(bias_loaded, 16)

            act.wait_ge(bias_loaded, 16 * BIAS_DMAS)

            def tower_pieces(pairs, halves):
                pieces = [(p, h) for p in pairs for h in halves]
                tower_hidden(pieces)
                tower_features(pieces)

            def tower_hidden(pieces):
                for p, h in pieces:
                    act.wait_ge(transposed, NH * p + h + 1)
                    nc.scalar.copy(tower_in_t[:, p, cols(h)], psum[:, tower_bank(p, h), :]).then_inc(in_t_ready[h], 1)
                for p, h in pieces:
                    act.wait_ge(layer1_done, NH * p + h + 1)
                    nc.scalar.activation(hidden[:, p, cols(h)], psum[:, tower_bank(p, h), :], ACT.Relu,
                                         bias=bias1[:, p:p + 1]).then_inc(hidden_ready[h], 1)

            def tower_features(pieces):
                for p, h in pieces:
                    act.wait_ge(layer2_done, NH * p + h + 1)
                    nc.scalar.activation(feat[block_lanes(p), p // 2, cols(h)],
                                         psum[0:2 * S_OUT, tower_bank(p, h), :], ACT.Identity,
                                         bias=bias2[:, p:p + 1]).then_inc(feat_ready[h], 1)

            def store_features(p):
                for h in range(NH):
                    act.wait_ge(feat_ready[h], p + 1)
                act.dma_start(feat_rows(64 * p, [[1, 64]]), feat[block_lanes(p), p // 2, :]
                              ).then_inc(feat_stored[p], 16)

            tower_hidden([(0, 0)])
            for n in range(2):
                act.wait_ge(seed_done, n + 1)
                nc.scalar.activation(cur[:, n, cols(0)], psum[:, SEED_BANK + n, :], ACT.Identity,
                                     bias=bias_lane[:, n:n + 1]).then_inc(seeded, 1)
            tower_features([(0, 0)])
            store_features(0)

            def split_heads(step, parity, slot, weights, count, tiles=2, reused=True):
                if reused:
                    act.wait_ge(steps_done, step - 1)
                act.wait_ge(weights, count)
                nc.scalar.copy(w_head[:, parity, 0:tiles, :], w_ij[:, slot, 0:tiles, :]).then_inc(w_head_ready, 1)
                act.wait_ge(prod_ready, step + 1)
                nc.scalar.copy(x_head[:, parity, 0:tiles, :], prod[:, parity, 0:tiles, :]).then_inc(x_head_ready, 1)

            second = [(1, h) for h in range(NH)]
            tower_hidden(second)
            split_heads(0, 0, 0, w_summed, 1, reused=False)
            tower_features(second)
            store_features(1)
            for step in range(1, PARK_AFTER + 1):
                split_heads(step, step % 2, step % W_RING, w_summed, step + 1, reused=step >= 2)
            for n in range(4):
                act.wait_ge(bank_closed, n + 1)
                nc.scalar.copy(parked[:, n, :], psum[:, 4 + n, :]).then_inc(bank_parked, 1)
            tower_pieces(range(N_EARLY, PAIRS), range(NH))
            for p in range(N_EARLY, PAIRS):
                store_features(p)
            for step in range(PARK_AFTER + 1, 2 * W_RING):
                split_heads(step, step % 2, step % W_RING, w_summed, step + 1)
            with act.Fori(2, SQUARES // W_RING) as it:
                for slot in range(W_RING):
                    split_heads(it * W_RING + slot, slot % 2, slot, w_summed, it * W_RING + slot + 1)
            for step in range(SQUARES // W_RING * W_RING, SQUARES):
                split_heads(step, step % 2, step % W_RING, w_summed, step + 1)
            split_heads(SQUARES, SQUARES % 2, SQUARES % W_RING, w_loaded[SQUARES % W_RING],
                        SQUARES // W_RING * W_DMAS + 2 * 16)
            split_heads(LAST, LAST % 2, LAST % W_RING, w_summed, LAST, tiles=1)

            act.wait_ge(head_loaded, 48)
            for n, bank in enumerate(END_ORDER):
                if bank >= 4:
                    act.wait_ge(bank_summed, n + 1)
                    ins = nc.scalar.activation(hidden[:, bank // NH, cols(bank % NH)], summed[:, bank - 4, :], ACT.Relu)
                else:
                    act.wait_ge(bank_done, n + 1)
                    ins = nc.scalar.activation(hidden[:, bank // NH, cols(bank % NH)], psum[:, bank, :], ACT.Relu,
                                               bias=head_b1[:, bank // NH:bank // NH + 1])
                ins.then_inc(bank_relu, 1)
            for h in range(NH):
                act.wait_ge(logits_done, h + 1)
                half_tiles = HALF // P
                nc.scalar.activation(
                    result[0:1, :].rearrange("a (p t) -> a t p", t=BT)[:, h * half_tiles:(h + 1) * half_tiles, :],
                    psum[0:1, 4 + h, :].rearrange("a (t p) -> a t p", p=P), ACT.Sigmoid, bias=head_b2[0:1, 0:1]
                ).then_inc(result_ready, 1)

        @block.vector
        def _(dve):
            chain = [0]

            def link(ins):
                chain[0] += 1
                ins.then_inc(dve_step, 1)
                dve.wait_ge(dve_step, chain[0])

            v = nc.vector
            v.memset(ones[:], 1.0).then_inc(ones_ready, 1)
            link(v.memset(tower_in[:, :, 0, :], 0.0))
            dve.wait_ge(tok_loaded, 16)
            dve.wait_ge(pool_consts, 1)
            link(v.tensor_tensor(tok_bad[:], tok[:], tok_want[:], ALU.not_equal))
            v.reduce_max(tok_bad_any[:], tok_bad[:], AX_X).then_inc(tok_checked, 1)
            dve.wait_ge(query_loaded, 16)
            link(v.tensor_scalar(valid[:], query[:], 0.0, None, ALU.is_ge))
            link(v.scalar_tensor_tensor(out=valid[:], in0=query[:], scalar=float(CARD - 1), in1=valid[:],
                                        op0=ALU.is_le, op1=ALU.mult))
            link(v.tensor_tensor(found[:], query[:], valid[:], ALU.mult))
            dve.wait_ge(bad_summed, 1)
            v.tensor_copy(bad_count[:], psum[0:1, 0, 0:1]).then_inc(bad_ready, 1)
            dve.wait_ge(bad_ready, 1)
            bad = dve.value_load(bad_count[0:1, 0:1], min_val=0, max_val=TOK_P)
            with dve.If(bad > 0):
                gen = [0]

                def glink(ins):
                    gen[0] += 1
                    ins.then_inc(gen_step, 1)
                    dve.wait_ge(gen_step, gen[0])

                dve.wait_ge(pool_consts, 3)
                glink(v.tensor_single_scalar(query_hi[:], query[:], 16, ALU.arith_shift_right))
                glink(v.tensor_single_scalar(query_lo[:], query[:], 0xFFFF, ALU.bitwise_and))
                glink(v.tensor_copy(query_hi_f[:], query_hi[:]))
                glink(v.tensor_copy(query_lo_f[:], query_lo[:]))
                glink(v.tensor_copy(rank, rank_i[:]))
                glink(v.memset(best[:], 0.0))
                before, per_chunk = gen[0], 2 + 3 * Q + 2
                hi_f = query_hi_f[:].rearrange("p t f -> p (t f)")
                lo_f = query_lo_f[:].rearrange("p t f -> p (t f)")
                with dve.Fori(0, N_CHUNKS) as ch:
                    inner = [0]

                    def clink(ins):
                        inner[0] += 1
                        ins.then_inc(gen_step, 1)
                        dve.wait_ge(gen_step, ch * per_chunk + (before + inner[0]))

                    dve.wait_ge(chunk_loaded, ch * 16 + 16)
                    clink(v.tensor_single_scalar(tok_hi, tok_all[:], 16, ALU.arith_shift_right))
                    clink(v.tensor_single_scalar(tok_lo, tok_all[:], 0xFFFF, ALU.bitwise_and))
                    for q in range(Q):
                        clink(v.scalar_tensor_tensor(out=match, in0=tok_lo, scalar=lo_f[:, q:q + 1],
                                                     in1=rank, op0=ALU.is_equal, op1=ALU.mult))
                        clink(v.scalar_tensor_tensor(out=match, in0=tok_hi, scalar=hi_f[:, q:q + 1],
                                                     in1=match, op0=ALU.is_equal, op1=ALU.mult))
                        clink(v.reduce_max(chunk_best[:, q:q + 1], match, AX_X))
                    clink(v.tensor_tensor(best[:], best[:], chunk_best[:], ALU.max))
                    clink(v.tensor_scalar(rank, rank, -float(CHUNK), None, ALU.add))
                    assert inner[0] == per_chunk
                    dve.sem_inc(chunk_used, 1)
                end = before + per_chunk * N_CHUNKS
                best3 = best[:].rearrange("p (t f) -> p t f", f=F)
                for n, ins in enumerate((
                    lambda: v.tensor_scalar(valid[:], best3, 0.0, None, ALU.is_gt),
                    lambda: v.tensor_scalar(found[:], best3, -1.0, float(CARD), ALU.mult, ALU.add),
                    lambda: v.tensor_tensor(found[:], found[:], valid[:], ALU.mult),
                )):
                    ins().then_inc(gen_step, 1)
                    dve.wait_ge(gen_step, end + n + 1)
            dve.wait_ge(pool_consts, 2)
            v.tensor_tensor(row[:], found[:], table_start[:], ALU.add).then_inc(rows_ready, 1)
            dve.wait_ge(dense_loaded, 16)
            v.tensor_copy(tower_in[:, :, 0, 0:D_DENSE], dense_in[:]).then_inc(dense_placed, 1)

            dve.wait_ge(w2_loaded, (F + 1) * 16)
            v.tensor_copy(w2_lane[:, 0, :].rearrange("p (r q) -> p r q", r=S_OUT),
                          w2[:, 0, S_OUT:2 * S_OUT].unsqueeze(2).to_broadcast([P, S_OUT, P // S_OUT])
                          ).then_inc(w2_lane_ready, 1)
            v.tensor_copy(w2_lane[:, 1, :].rearrange("p (q r) -> p q r", r=S_OUT),
                          w2[:, 0, 0:S_OUT].unsqueeze(1).to_broadcast([P, P // S_OUT, S_OUT])
                          ).then_inc(w2_lane_ready, 1)
            dve.wait_ge(bias_loaded, 16 * BIAS_DMAS)
            h, bank = 1, tower_bank(0, 1)
            dve.wait_ge(transposed, h + 1)
            v.tensor_copy(tower_in_t[:, 0, cols(h)], psum[:, bank, :]).then_inc(in_t_ready[h], 1)
            dve.wait_ge(layer1_done, h + 1)
            v.tensor_scalar(hidden[:, 0, cols(h)], psum[:, bank, :], bias1[:, 0:1], 0.0, ALU.add, ALU.max
                            ).then_inc(hidden_ready[h], 1)
            for n in range(2):
                dve.wait_ge(seed_done, 2 * h + n + 1)
                v.tensor_scalar(cur[:, n, cols(h)], psum[:, SEED_BANK + 2 * h + n, :], bias_lane[:, n:n + 1], None,
                                ALU.add).then_inc(seeded, 1)
            dve.wait_ge(layer2_done, h + 1)
            v.tensor_scalar(feat[block_lanes(0), 0, cols(h)], psum[0:2 * S_OUT, bank, :], bias2[:, 0:1], None, ALU.add
                            ).then_inc(feat_ready[h], 1)

            def start_round(r):
                dve.wait_ge(staged_loaded, r * ST_DMAS)
                v.tensor_copy(cur[:].rearrange("p a n -> p (a n)"), staged[:].rearrange("p a n -> p (a n)")
                              ).then_inc(staged_free, 1)
                dve.wait_ge(staged_free, r)

            def sum_weights(slot, use):
                flat = "p u n -> p (u n)"
                dve.wait_ge(w_loaded[slot], use * W_DMAS + W_DMAS)
                v.tensor_tensor(w_ij[:, slot].rearrange(flat), w_ij[:, slot].rearrange(flat),
                                w_ji[:, slot].rearrange(flat), ALU.add).then_inc(w_summed, 1)

            def spread_lower(kind, t, parity):
                for u in range(2):
                    ins = v.stream_shuffle(prod[:, parity, u, :], cur[:, 1, :], spread_mask(kind, t + u))
                ins.then_inc(lower_spread, 1)

            def multiply(step, parity):
                dve.wait_ge(lower_spread, step + 1)
                v.tensor_tensor(prod[:, parity], prod[:, parity],
                                cur[:, 0:1, :].to_broadcast([P, 2, B]), ALU.mult).then_inc(prod_ready, 1)

            def weight_tails(step, parity, slot, tiles=2):
                dve.wait_ge(w_head_ready, step + 1)
                v.tensor_tensor(w_tail[:, parity, 0:tiles, :], w_ij[:, slot, 0:tiles, :],
                                w_head[:, parity, 0:tiles, :].bitcast(F32), ALU.subtract).then_inc(w_tail_ready, 1)

            def product_tails(step, parity, tiles=2):
                dve.wait_ge(x_head_ready, step + 1)
                v.tensor_tensor(x_tail[:, parity, 0:tiles, :], prod[:, parity, 0:tiles, :],
                                x_head[:, parity, 0:tiles, :].bitcast(F32), ALU.subtract).then_inc(x_tail_ready, 1)

            def round_steps(kind, n, r, number, first):
                for s in range(n):
                    step = r * n + (first + s)
                    if s == 0:
                        if number is None:
                            dve.wait_ge(seeded, 2 * NH)
                        else:
                            start_round(number)
                    sum_weights(s % W_RING, r * (n // W_RING) + (first + s) // W_RING)
                    if s:
                        if s >= 2:
                            dve.wait_ge(x_tail_ready, r * n + (first + s - 1))
                        weight_tails(r * n + (first + s - 1), (s - 1) % 2, (s - 1) % W_RING)
                    spread_lower(kind, 2 * s, s % 2)
                    if s:
                        product_tails(r * n + (first + s - 1), (s - 1) % 2)
                    multiply(step, s % 2)
                weight_tails(r * n + (first + n - 1), 1, W_RING - 1)
                product_tails(r * n + (first + n - 1), 1)
                dve.wait_ge(prod_ready, r * n + (first + n))
                dve.wait_ge(x_tail_ready, r * n + (first + n))

            def looped_rounds(kind, n_rounds, n, first_round, first):
                with dve.Fori(0, n_rounds) as r:
                    round_steps(kind, n, r, r + first_round, first)

            round_steps((BLOCK, 32), BLOCK_STEPS, 0, None, 0)
            looped_rounds((BLOCK, 32), N_BLOCKS - 1, BLOCK_STEPS, 1, BLOCK_STEPS)
            looped_rounds((GROUP, 64), 4, 8, N_BLOCKS, FIRST_64)
            looped_rounds((GROUP, 128), 4, 16, N_BLOCKS + 4, FIRST_128)
            step = FIRST_TAIL
            for number, (kind, _k, n) in enumerate(TAIL[:-1], TAIL_ROUND):
                dve.wait_ge(prod_ready, step)
                start_round(number)
                for s in range(n):
                    sum_weights(step % W_RING, step // W_RING)
                    if step > FIRST_TAIL:
                        weight_tails(step - 1, (step - 1) % 2, (step - 1) % W_RING)
                    dve.wait_ge(x_tail_ready, step - 1)
                    spread_lower(kind, 2 * s, step % 2)
                    if step > FIRST_TAIL:
                        product_tails(step - 1, (step - 1) % 2)
                    multiply(step, step % 2)
                    step += 1
            dve.wait_ge(x_tail_ready, SQUARES - 1)
            v.tensor_tensor(prod[:, SQUARES % 2], feat[:], feat[:], ALU.mult).then_inc(prod_ready, 1)
            weight_tails(SQUARES - 1, (SQUARES - 1) % 2, (SQUARES - 1) % W_RING)
            product_tails(SQUARES - 1, (SQUARES - 1) % 2)
            dve.wait_ge(prod_ready, LAST)
            start_round(len(ROUNDS) - 1)
            dve.wait_ge(w_loaded[LAST % W_RING], LAST // W_RING * W_DMAS + 2 * 16)
            v.tensor_tensor(w_ij[:, LAST % W_RING, 0, :], w_ij[:, LAST % W_RING, 0, :],
                            w_ji[:, LAST % W_RING, 0, :], ALU.add).then_inc(w_summed, 1)
            dve.wait_ge(x_tail_ready, LAST - 1)
            v.tensor_tensor(prod[:, LAST % 2, 0, :], cur[:, 0, :], cur[:, 1, :], ALU.mult).then_inc(prod_ready, 1)
            weight_tails(SQUARES, SQUARES % 2, SQUARES % W_RING)
            product_tails(SQUARES, SQUARES % 2)
            weight_tails(LAST, LAST % 2, LAST % W_RING, tiles=1)
            product_tails(LAST, LAST % 2, tiles=1)

            dve.wait_ge(head_loaded, 48)
            for n in range(4):
                dve.wait_ge(bank_done, n + 1)
                nt = (4 + n) // NH
                v.scalar_tensor_tensor(out=summed[:, n, :], in0=psum[:, 4 + n, :], scalar=head_b1[:, nt:nt + 1],
                                       in1=parked[:, n, :], op0=ALU.add, op1=ALU.add).then_inc(bank_summed, 1)
            for n, bank in enumerate(END_ORDER):
                nt, h = bank // NH, bank % NH
                dve.wait_ge(bank_relu, n + 1)
                if n < NH:
                    ins = v.tensor_scalar(score[:, h, :], hidden[:, nt, cols(h)], head_w2[:, nt:nt + 1], None, ALU.mult)
                else:
                    dve.wait_ge(score_step, n - 1)
                    ins = v.scalar_tensor_tensor(out=score[:, h, :], in0=hidden[:, nt, cols(h)],
                                                 scalar=head_w2[:, nt:nt + 1], in1=score[:, h, :],
                                                 op0=ALU.mult, op1=ALU.add)
                ins.then_inc(score_step, 1)

        @block.tensor
        def _(pe):
            pe.wait_ge(tok_checked, 1)
            pe.matmul(psum[0:1, 0, 0:1], tok_bad_any[:], ones[0:TOK_P, :], start=True, stop=True
                      ).then_inc(bad_summed, 1)
            pe.wait_ge(pool_consts, 5)
            pe.wait_ge(bad_ready, 1)
            pe.wait_ge(dense_placed, 1)
            pe.wait_ge(w1_loaded, 3 * 16)
            pe.wait_ge(w2_loaded, (F + 1) * 16)
            pe.wait_ge(w2_lane_ready, 2)

            def towers(pairs):
                pieces = [(p, h) for p in pairs for h in range(NH)]
                for p, h in pieces:
                    if h == 0:
                        pe.wait_ge(gathered[p], (1 if p == 0 else 2) * BT * 16)
                    if p >= N_EARLY:
                        pe.wait_ge(bank_parked, tower_bank(p, h) - 3)
                    for t in range(BT // NH):
                        slots = tower_in[:, h * BT // NH + t, 2 * p:2 * p + 2, :].rearrange("p s e -> p (s e)")
                        ins = pe.transpose(psum[:, tower_bank(p, h), t * P:(t + 1) * P], slots, ident[:])
                    ins.then_inc(transposed, 1)
                for p, h in pieces:
                    pe.wait_ge(in_t_ready[h], p + 1)
                    pe.matmul(psum[:, tower_bank(p, h), :], w1[:, p, :], tower_in_t[:, p, cols(h)],
                              start=True, stop=True).then_inc(layer1_done, 1)
                for p, h in pieces:
                    pe.wait_ge(hidden_ready[h], p + 1)
                    if p == 0:
                        for n in range(2):
                            pe.matmul(psum[:, SEED_BANK + 2 * h + n, :], w2_lane[:, n, :], hidden[:, 0, cols(h)],
                                      start=True, stop=True).then_inc(seed_done, 1)
                for p, h in pieces:
                    pe.matmul(psum[0:2 * S_OUT, tower_bank(p, h), :], w2[:, p, :], hidden[:, p, cols(h)],
                              start=True, stop=True).then_inc(layer2_done, 1)

            TERMS = ((w_head, x_head), (w_tail, x_head), (w_head, x_tail))

            def product(bank, term, parity, u, start=False, stop=False):
                nt, h = bank // NH, bank % NH
                w, x = TERMS[term]
                return pe.matmul(psum[:, bank, :], w[:, parity, u, nt * P:(nt + 1) * P], x[:, parity, u, cols(h)],
                                 start=start, stop=stop)

            def step_products(step, parity, fresh=()):
                pe.wait_ge(w_head_ready, step + 1)
                pe.wait_ge(x_head_ready, step + 1)
                for u in range(2):
                    for bank in range(8):
                        product(bank, 0, parity, u, start=bank in fresh and u == 0)
                pe.wait_ge(w_tail_ready, step + 1)
                for u in range(2):
                    for bank in range(8):
                        product(bank, 1, parity, u)
                pe.wait_ge(x_tail_ready, step + 1)
                for u in range(2):
                    for bank in range(8):
                        ins = product(bank, 2, parity, u)
                ins.then_inc(steps_done, 1)

            for p in range(N_EARLY):
                towers([p])
            for h in range(NH):
                pe.wait_ge(feat_ready[h], N_EARLY)
            pe.wait_ge(seeded, 2 * NH)
            step_products(0, 0, fresh=range(8))
            for step in range(1, PARK_AFTER - 1):
                step_products(step, step % 2)
            step, parity = PARK_AFTER - 1, (PARK_AFTER - 1) % 2
            pe.wait_ge(w_tail_ready, step + 1)
            pe.wait_ge(x_tail_ready, step + 1)
            for bank in END_ORDER:
                for term in range(3):
                    for u in range(2):
                        ins = product(bank, term, parity, u, stop=bank >= 4 and term == 2 and u == 1)
                if bank >= 4:
                    ins.then_inc(bank_closed, 1)
            ins.then_inc(steps_done, 1)
            towers(range(N_EARLY, PAIRS))
            for h in range(NH):
                pe.wait_ge(feat_ready[h], PAIRS)
            step_products(PARK_AFTER, PARK_AFTER % 2, fresh=range(4, 8))
            step_products(PARK_AFTER + 1, (PARK_AFTER + 1) % 2)
            with pe.Fori(PARK_AFTER // 2 + 1, SQUARES // 2) as it:
                for parity in range(2):
                    step_products(it * 2 + parity, parity)
            step_products(SQUARES - 1, (SQUARES - 1) % 2)
            pe.wait_ge(w_tail_ready, SQUARES + 1)
            pe.wait_ge(x_tail_ready, SQUARES + 1)
            for bank in END_ORDER:
                for term in range(3):
                    product(bank, term, SQUARES % 2, 0)
            pe.wait_ge(w_tail_ready, LAST + 1)
            pe.wait_ge(x_tail_ready, LAST + 1)
            for bank in END_ORDER:
                for parity, u in ((SQUARES % 2, 1), (LAST % 2, 0)):
                    for term in range(3):
                        ins = product(bank, term, parity, u, stop=parity == LAST % 2 and term == 2)
                ins.then_inc(bank_done, 1)
            for h in range(NH):
                pe.wait_ge(score_step, 2 * NT - NH + h + 1)
                pe.matmul(psum[0:1, 4 + h, :], ones[:], score[:, h, :], start=True, stop=True).then_inc(logits_done, 1)


_INS = ["r_dense_features", "r_sparse_features", "L0_rec_tokenizers", "L0_rec_emb_tables", "L0_rec_dw1",
        "L0_rec_db1", "L0_rec_dw2", "L0_rec_db2", "L0_rec_sw1", "L0_rec_sb1", "L0_rec_sw2", "L0_rec_sb2",
        "L0_rec_pw1", "L0_rec_pb1", "L0_rec_pw2", "L0_rec_pb2"]


def kernel(**inputs):
    import numpy as np
    import concourse.bacc as bacc
    from concourse.bass_utils import run_bass_kernel_spmd

    nc = bacc.Bacc("TRN2", target_bir_lowering=False, num_devices=1)
    arrays, args = {}, []
    for name in _INS:
        a = np.ascontiguousarray(inputs[name])
        arrays[f"in_{name}"] = a
        args.append(nc.dram_tensor(f"in_{name}", a.shape, mybir.dt.from_np(a.dtype), kind="ExternalInput").ap())
    out = nc.dram_tensor("out_probability", (arrays["in_r_dense_features"].shape[0],), F32, kind="ExternalOutput").ap()
    rec_kernel(nc, *args, out)
    r = run_bass_kernel_spmd(nc, [arrays], core_ids=[0])
    return r.results[0]["out_probability"]
```
